# Optimizing a Trainium2 kernel written in Bass

```python
import numpy as np
import jax
import jax.numpy as jnp

def _softmax(x, axis=-1):
    return jax.nn.softmax(x, axis=axis)

def _gelu(x):
    return jax.nn.gelu(x, approximate=True)

def _silu(x):
    return jax.nn.silu(x)

def _sigmoid(x):
    return jax.nn.sigmoid(x)

def _layernorm(x, axis=-1, eps=1e-05):
    m = jnp.mean(x, axis=axis, keepdims=True)
    v = jnp.var(x, axis=axis, keepdims=True)
    return (x - m) / jnp.sqrt(v + eps)

def _scatter_add(tgt, idx, src, axis=0):
    return tgt.at[idx].add(src)

def _segment_sum(src, seg, n):
    return jax.ops.segment_sum(src, seg, n)
kernel_name = 'mk_macaron_d1_jaxref_r4_429858'

def setup_inputs(seed: int=0):
    np.random.seed(seed)
    _w = jnp.asarray

    def _L0_attn_setup():
        import jax, jax.numpy as jnp
        import numpy as np

        def _sin_rpe(Lq, d_model, dtype):
            inv_freq = 1.0 / 10000.0 ** (jnp.arange(0, d_model, 2, dtype=jnp.float32) / d_model)
            pos = jnp.arange(-(Lq - 1), Lq, dtype=jnp.float32)
            ang = pos[:, None] * inv_freq[None, :]
            emb = jnp.zeros((2 * Lq - 1, d_model), dtype=jnp.float32)
            emb = emb.at[:, 0::2].set(jnp.sin(ang)).at[:, 1::2].set(jnp.cos(ang))
            return emb.astype(dtype)

        def _rel_shift(x):
            B, H, Lq, Lr = x.shape
            xp = jnp.concatenate([jnp.zeros((B, H, Lq, 1), x.dtype), x], axis=-1)
            xp = xp.reshape(B, H, Lr + 1, Lq)
            return xp[:, :, 1:].reshape(B, H, Lq, Lr)[..., Lr - Lq:]
        key = jax.random.key(seed)
        ks = jax.random.split(key, 7)
        B, Lq, D, H = (1, 512, 256, 16)
        d_head = D // H
        s = 0.02
        return {'w': jax.random.normal(ks[0], (B, Lq, D), jnp.float32), 'Wq': jax.random.normal(ks[1], (D, D), jnp.float32) * s, 'Wk': jax.random.normal(ks[2], (D, D), jnp.float32) * s, 'Wv': jax.random.normal(ks[3], (D, D), jnp.float32) * s, 'Wr': jax.random.normal(ks[4], (D, D), jnp.float32) * s, 'u_bias': jax.random.normal(ks[5], (H, d_head), jnp.float32) * 0.02, 'v_bias': jax.random.normal(ks[6], (H, d_head), jnp.float32) * 0.02}
    _L0_attn_in = _L0_attn_setup()

    def _L0_ffn_setup():
        import jax, jax.numpy as jnp
        import numpy as np
        TOP_K = 2
        key = jax.random.key(seed)
        k1, k2, k3, k4 = jax.random.split(key, 4)
        B_, S, D = (4, 2048, 256)
        E, R = (8, 16)
        x = jax.random.normal(k1, (B_, S, D), dtype=jnp.float32)
        Wg = jax.random.normal(k2, (D, E), dtype=jnp.float32) * 0.02
        A = jax.random.normal(k3, (E, D, R), dtype=jnp.float32) * 0.02
        Bm = jax.random.normal(k4, (E, R, D), dtype=jnp.float32) * 0.02
        return {'x': x, 'Wg': Wg, 'A': A, 'B': Bm}
    _L0_ffn_in = _L0_ffn_setup()
    _d = {'L0_attn_w': _L0_attn_in['w'], 'L0_attn_Wq': _L0_attn_in['Wq'], 'L0_attn_Wk': _L0_attn_in['Wk'], 'L0_attn_Wv': _L0_attn_in['Wv'], 'L0_attn_Wr': _L0_attn_in['Wr'], 'L0_attn_u_bias': _L0_attn_in['u_bias'], 'L0_attn_v_bias': _L0_attn_in['v_bias'], 'L0_ffn_Wg': _L0_ffn_in['Wg'], 'L0_ffn_A': _L0_ffn_in['A'], 'L0_ffn_B': _L0_ffn_in['B']}
    _x0 = _d['L0_attn_w']
    _d['L0_attn_w'] = jax.random.normal(jax.random.fold_in(jax.random.key(seed), 1), (2, 2048, 256), dtype=_x0.dtype)
    del _x0
    return _d

def reference(L0_attn_w, L0_attn_Wq, L0_attn_Wk, L0_attn_Wv, L0_attn_Wr, L0_attn_u_bias, L0_attn_v_bias, L0_ffn_Wg, L0_ffn_A, L0_ffn_B):

    def _L0_attn_ref(w, Wq, Wk, Wv, Wr, u_bias, v_bias):
        import jax, jax.numpy as jnp
        import numpy as np

        def _sin_rpe(Lq, d_model, dtype):
            inv_freq = 1.0 / 10000.0 ** (jnp.arange(0, d_model, 2, dtype=jnp.float32) / d_model)
            pos = jnp.arange(-(Lq - 1), Lq, dtype=jnp.float32)
            ang = pos[:, None] * inv_freq[None, :]
            emb = jnp.zeros((2 * Lq - 1, d_model), dtype=jnp.float32)
            emb = emb.at[:, 0::2].set(jnp.sin(ang)).at[:, 1::2].set(jnp.cos(ang))
            return emb.astype(dtype)

        def _rel_shift(x):
            B, H, Lq, Lr = x.shape
            xp = jnp.concatenate([jnp.zeros((B, H, Lq, 1), x.dtype), x], axis=-1)
            xp = xp.reshape(B, H, Lr + 1, Lq)
            return xp[:, :, 1:].reshape(B, H, Lq, Lr)[..., Lr - Lq:]
        B, Lq, D = w.shape
        H, d_head = u_bias.shape
        scale = 1.0 / np.sqrt(d_head).astype(np.float32)
        r = _sin_rpe(Lq, D, w.dtype)
        q = (w @ Wq.T).reshape(B, Lq, H, d_head).transpose(0, 2, 1, 3)
        k = (w @ Wk.T).reshape(B, Lq, H, d_head).transpose(0, 2, 1, 3)
        v = (w @ Wv.T).reshape(B, Lq, H, d_head).transpose(0, 2, 1, 3)
        rp = (r @ Wr.T).reshape(2 * Lq - 1, H, d_head).transpose(1, 0, 2)
        AC = jnp.einsum('bhid,bhjd->bhij', q + u_bias[None, :, None, :], k)
        BD = jnp.einsum('bhid,hjd->bhij', q + v_bias[None, :, None, :], rp)
        BD = _rel_shift(BD)
        attn = jax.nn.softmax((AC + BD) * scale, axis=-1)
        out = jnp.einsum('bhij,bhjd->bhid', attn, v)
        return out.transpose(0, 2, 1, 3).reshape(B, Lq, D)

    def _L0_ffn_ref(x, Wg, A, B):
        import jax, jax.numpy as jnp
        import numpy as np
        TOP_K = 2
        D = x.shape[-1]
        E = Wg.shape[-1]
        xs = x.reshape(-1, D)
        gate_logits = xs @ Wg
        topw, sel = jax.lax.top_k(gate_logits, TOP_K)
        topw = jax.nn.softmax(topw.astype(jnp.float32), axis=-1).astype(x.dtype)
        cw = jnp.sum(jax.nn.one_hot(sel, E, dtype=x.dtype) * topw[..., None], axis=1)
        h = jnp.einsum('td,edr->ter', xs, A)
        hw = h * cw[..., None]
        out = jnp.einsum('ter,erd->td', hw, B)
        return out.reshape(x.shape)
    x = L0_attn_w
    x = x + 0.5 * _L0_ffn_ref(_layernorm(x, axis=-1), L0_ffn_Wg, L0_ffn_A, L0_ffn_B)
    x = x + _L0_attn_ref(_layernorm(x, axis=-1), L0_attn_Wq, L0_attn_Wk, L0_attn_Wv, L0_attn_Wr, L0_attn_u_bias, L0_attn_v_bias)
    x = x + 0.5 * _L0_ffn_ref(_layernorm(x, axis=-1), L0_ffn_Wg, L0_ffn_A, L0_ffn_B)
    return x

_drawn_inputs = setup_inputs


def setup_inputs(seed=0):
    import zlib

    import numpy as np

    out = dict(_drawn_inputs(seed))
    spreads = {}
    factors = {'L0_attn_Wq': 8.0,
     'L0_attn_Wk': 8.0,
     'L0_attn_Wv': 7.583,
     'L0_attn_Wr': 8.0,
     'L0_attn_u_bias': 8.0,
     'L0_attn_v_bias': 8.0,
     'L0_ffn_Wg': 3.617,
     'L0_ffn_A': 3.114,
     'L0_ffn_B': 3.123}
    for name, (base, spread) in spreads.items():
        noise = np.random.default_rng([zlib.crc32(name.encode()), seed]).standard_normal(out[name].shape)
        drawn = base * np.exp(spread * noise) if base else spread * noise
        out[name] = jnp.asarray(drawn.astype(out[name].dtype))
    for name, factor in factors.items():
        out[name] = (out[name] * factor).astype(out[name].dtype)
    return out
```

```python
from contextlib import ExitStack

import concourse.bass as bass
from concourse import mybir

ALU = mybir.AluOpType
ACT = mybir.ActivationFunctionType
AX = mybir.AxisListType
F32 = mybir.dt.float32
BF16 = mybir.dt.bfloat16
U32 = mybir.dt.uint32

P = 128
Q_PARTS = (0, 0, 0, 1, 1, 2)
K_PARTS = (0, 1, 2, 0, 1, 0)
EPS = 1e-5


def build_program(nc, x, wq_t, wk_t, wv_t, wr_t, u_bias, v_bias, w_in, w_out, pos_t, ident, fold, iota, out):
    NB, L, D = x.shape
    E = iota.shape[2]
    ER = w_out.shape[0]
    R = ER // E
    H, DH = 16, D // 16
    KT = D // P
    NI = L // P
    NPOS = 2 * L
    WIN = L + P
    TG = 4
    GT = TG * P
    GB = L // GT
    NG = NB * GB
    HEADS = NB * H
    STACK = len(Q_PARTS) * DH
    VW = 32
    SCALE = float(DH) ** -0.5
    NEG = -3.0e38
    BANK = 512
    assert (P, D, DH, KT, ER) == (128, 256, 16, 2, 128)

    ctx = ExitStack()
    with ctx:
        def sb(name, shape, dt=F32):
            return ctx.enter_context(nc.sbuf_tensor(name, shape, dt))

        def sem(name):
            return ctx.enter_context(nc.semaphore(name))

        bank = [ctx.enter_context(nc.psum_tensor(f"bank{i}", [P, BANK], F32)) for i in range(8)]

        qu_parts = nc.dram_tensor("qu_parts", (3, HEADS * DH, L), BF16, kind="Internal").ap()
        qv_parts = nc.dram_tensor("qv_parts", (3, HEADS * DH, L), BF16, kind="Internal").ap()
        k_parts = nc.dram_tensor("k_parts", (3, HEADS * DH, L), BF16, kind="Internal").ap()
        pos_parts = nc.dram_tensor("pos_parts", (3, HEADS * DH, NPOS), BF16, kind="Internal").ap()
        v_heads = nc.dram_tensor("v_heads", (HEADS, P, NI * VW), F32, kind="Internal").ap()
        SLOTS = 4
        SCORES = 8
        shift_dram = nc.dram_tensor("shift_dram", (SLOTS, P, WIN), F32, kind="Internal")

        resid = sb("resid", [P, HEADS, NI, DH])
        ident_sb = sb("ident_sb", [P, P])
        fold_sb = sb("fold_sb", [P, VW])
        w_in_sb = sb("w_in_sb", [P, KT, E + ER])
        w_out_sb = sb("w_out_sb", [P, D])
        iota_sb = sb("iota_sb", [P, TG, E])
        w_loaded = sem("w_loaded")

        def resid_tile(b, q, t):
            return resid[:, bass.ds(b * H, H), q * TG + t, :]

        def by_head(ap):
            return ap.rearrange("p (h d) -> p h d", h=H)

        NORM_STEPS = 2 * TG + 1
        FFN_STEPS = NORM_STEPS + 3 * TG + 7

        def ffn_buffers(c, tag):
            def s(name, shape, dt=F32):
                return c.enter_context(nc.sbuf_tensor(f"{name}_{tag}", shape, dt))
            return dict(
                norm=s("normed", [P, TG, D]), norm_t=s("normed_t", [P, KT, GT]),
                stats=s("stats", [P, TG, 6]), mean_var=s("mean_var", [P, TG, 2]), rstd=s("rstd", [P, TG]),
                var=s("var", [P, TG]), root=s("root", [P, TG]),
                logits=s("logits", [P, TG, E]), top=s("top", [P, TG, 8]), top_i=s("top_i", [P, TG, 8], U32),
                top_f=s("top_f", [P, TG, 2]), diff=s("diff", [P, TG]), ex=s("ex", [P, TG]),
                den=s("den", [P, TG]), w=s("w_top", [P, 2, TG]), mask=s("mask", [P, 2, TG, E]),
                gate=s("gate", [P, TG, E]), hw=s("hw", [P, TG, ER]), hw_t=s("hw_t", [P, GT]))

        def ffn_sems(tag):
            names = ("var", "rooted", "normed", "norm_tp", "norm_t", "hidden", "diff", "exp", "gated", "gated_tp", "gated_t",
                     "ffn", "chain", "y")
            return {n: sem(f"{n}_{tag}") for n in names}

        def wait_apart(eng, semaphore, count):
            eng.wait_ge(semaphore, count)
            eng.nop(nofuse=True)

        def layer_norm(dve, B, S, base, no, tile, normed):
            chain = S["chain"]
            for t in range(TG):
                dve.bn_stats(B["stats"][:, t, :], tile(t)).then_inc(chain, 1)
            for t in range(TG):
                wait_apart(dve, chain, base + (t + 1))
                dve.bn_aggr(B["mean_var"][:, t, :], B["stats"][:, t, :]).then_inc(chain, 1)
            dve.wait_ge(chain, base + 2 * TG)
            dve.tensor_scalar(B["var"][:, :], B["mean_var"][:, :, 1], EPS, None, ALU.add).then_inc(S["var"], 1)
            dve.wait_ge(S["rooted"], no)
            dve.reciprocal(B["rstd"][:, :], B["root"][:, :]).then_inc(chain, 1)
            dve.wait_ge(chain, base + (2 * TG + 1))
            for t in range(TG):
                dve.tensor_scalar(by_head(B["norm"][:, t, :]), tile(t), B["mean_var"][:, t, 0:1],
                                  B["rstd"][:, t:t + 1], ALU.subtract, ALU.mult).then_inc(normed, 1)

        def pairs(i, width):
            return bank[i][:, 0:2 * width].rearrange("p (t c) -> p t c", t=2)

        def root(act, B, S, no):
            act.wait_ge(S["var"], no)
            act.activation(B["root"][:, :], B["var"][:, :], ACT.Sqrt).then_inc(S["rooted"], 1)

        def ffn_dve(dve, B, S, g, base, no, tile, y_tile, y_free=None):
            chain = S["chain"]
            layer_norm(dve, B, S, base, no, tile, S["normed"])
            n = base + NORM_STEPS
            dve.wait_ge(S["hidden"], g + 1)
            for i in range(2):
                dve.tensor_copy(B["logits"][:, 2 * i:2 * i + 2, :], pairs(2 + i, E + ER)[:, :, 0:E])\
                   .then_inc(chain, 1)
            wait_apart(dve, chain, n + 2)
            for t in range(TG):
                dve.max(B["top"][:, t, :], B["logits"][:, t, :]).then_inc(chain, 1)
            n = n + 2
            dve.wait_ge(chain, n + TG)
            dve.tensor_tensor(B["diff"][:, :], B["top"][:, :, 1], B["top"][:, :, 0], ALU.subtract)\
               .then_inc(S["diff"], 1)
            for t in range(TG):
                dve.max_index(B["top_i"][:, t, :], B["top"][:, t, :], B["logits"][:, t, :]).then_inc(chain, 1)
            n = n + 2 * TG
            dve.wait_ge(chain, n)
            dve.tensor_copy(B["top_f"][:, :, :], B["top_i"][:, :, 0:2]).then_inc(chain, 1)
            dve.wait_ge(S["exp"], g + 1)
            dve.tensor_scalar(B["den"][:, :], B["ex"][:, :], 2.0, 2.0, ALU.mult, ALU.add).then_inc(chain, 1)
            dve.wait_ge(chain, n + 2)
            dve.reciprocal(B["w"][:, 0, :], B["den"][:, :]).then_inc(chain, 1)
            for j in range(2):
                dve.tensor_tensor(B["mask"][:, j], iota_sb[:, :, :],
                                  B["top_f"][:, :, j:j + 1].to_broadcast([P, TG, E]), ALU.is_equal)\
                   .then_inc(chain, 1)
            dve.wait_ge(chain, n + 5)
            dve.tensor_tensor(B["w"][:, 1, :], B["w"][:, 0, :], B["ex"][:, :], ALU.mult).then_inc(chain, 1)
            dve.wait_ge(chain, n + 6)
            for j in range(2):
                wj = B["w"][:, j, :].rearrange("p (t o) -> p t o", o=1).to_broadcast([P, TG, E])
                dve.tensor_tensor(B["mask"][:, j], B["mask"][:, j], wj, ALU.mult).then_inc(chain, 1)
            dve.wait_ge(chain, n + 8)
            dve.tensor_tensor(B["gate"][:, :, :], B["mask"][:, 0], B["mask"][:, 1], ALU.add).then_inc(chain, 1)
            dve.wait_ge(chain, n + 9)
            for t in range(TG):
                dve.tensor_tensor(B["hw"][:, t, :].rearrange("p (e r) -> p e r", e=E),
                                  pairs(2 + t // 2, E + ER)[:, t % 2, E:E + ER]
                                  .rearrange("p (e r) -> p e r", e=E),
                                  B["gate"][:, t, :].rearrange("p (e o) -> p e o", o=1).to_broadcast([P, E, R]),
                                  ALU.mult).then_inc(S["gated"], 1)
            if y_free is not None:
                dve.wait_ge(y_free, 16 * (g + 1))
            dve.wait_ge(S["ffn"], g + 1)
            for t in range(TG):
                dve.tensor_tensor(y_tile(t), by_head(pairs(5 + t // 2, D)[:, t % 2, :]), tile(t), ALU.add)\
                   .then_inc(S["y"], 1)

        def ffn_act(act, B, S, g, no):
            root(act, B, S, no)
            for kt in range(KT):
                act.wait_ge(S["norm_tp"], g * KT + (kt + 1))
                act.copy(B["norm_t"][:, kt, :], bank[kt][:, :]).then_inc(S["norm_t"], 1)
            act.wait_ge(S["diff"], g + 1)
            act.activation(B["ex"][:, :], B["diff"][:, :], ACT.Exp).then_inc(S["exp"], 1)
            act.wait_ge(S["gated_tp"], g + 1)
            act.copy(B["hw_t"][:, :], bank[4][:, :]).then_inc(S["gated_t"], 1)

        def transpose_normed(pe, B, transposed):
            for kt in range(KT):
                for t in range(TG):
                    last = pe.matmul(bank[kt][:, t * P:(t + 1) * P], lhsT=B["norm"][:, t, kt * P:(kt + 1) * P],
                                     rhs=ident_sb[:, :], is_transpose=True, start=True, stop=True)
                last.then_inc(transposed, 1)

        def ffn_pe(pe, B, S, g):
            pe.wait_ge(S["normed"], g * TG + TG)
            transpose_normed(pe, B, S["norm_tp"])
            pe.wait_ge(S["norm_t"], g * KT + KT)
            for t in range(TG):
                for kt in range(KT):
                    last = pe.matmul(pairs(2 + t // 2, E + ER)[:, t % 2, :],
                                     lhsT=B["norm_t"][:, kt, t * P:(t + 1) * P], rhs=w_in_sb[:, kt, :],
                                     start=(kt == 0), stop=(kt == KT - 1))
            last.then_inc(S["hidden"], 1)
            pe.wait_ge(S["gated"], g * TG + TG)
            for t in range(TG):
                last = pe.matmul(bank[4][:, t * P:(t + 1) * P], lhsT=B["hw"][:, t, :], rhs=ident_sb[:, :],
                                 is_transpose=True, start=True, stop=True)
            last.then_inc(S["gated_tp"], 1)
            pe.wait_ge(S["gated_t"], g + 1)
            for t in range(TG):
                last = pe.matmul(pairs(5 + t // 2, D)[:, t % 2, :], lhsT=B["hw_t"][:, t * P:(t + 1) * P],
                                 rhs=w_out_sb[:, :], start=True, stop=True)
            last.then_inc(S["ffn"], 1)

        with ExitStack() as c1:
            B = ffn_buffers(c1, "one")
            S = ffn_sems("one")

            def s1(name, shape, dt=F32):
                return c1.enter_context(nc.sbuf_tensor(name, shape, dt))
            x_all = s1("x_all", [P, NB * NI, D])
            wq_sb, wk_sb, wv_sb, wr_sb = (s1(n, [P, KT, D]) for n in ("wq_sb", "wk_sb", "wv_sb", "wr_sb"))
            bias_sb = s1("bias_sb", [P, 2, KT])
            pos_sb = s1("pos_sb", [P, 2, KT, BANK])
            v_sb = s1("v_sb", [P, H, TG, VW])
            NPJ = 2 * KT
            NSPLIT = 3 * KT
            proj = s1("proj", [P, NPJ, BANK])
            part = s1("part", [P, NSPLIT, 3, BANK], BF16)
            rest = s1("rest", [P, NSPLIT, BANK])
            NPC = NPOS // BANK
            NPS = KT * NPC
            NSTEP = NORM_STEPS + FFN_STEPS
            x_loaded = sem("x_loaded")
            pos_loaded = [sem(f"pos_loaded{i}") for i in range(2)]
            normed2, norm2_tp, norm2_t = sem("normed2"), sem("norm2_tp"), sem("norm2_t")
            projected, proj_out, v_projected, v_out = sem("projected"), sem("proj_out"), sem("v_proj"), sem("v_out")
            part1, rest1, part2, part3 = sem("part1"), sem("rest1"), sem("part2"), sem("part3")
            stored = [sem(f"stored{i}") for i in range(NSPLIT)]
            v_padded, v_stored = sem("v_padded"), sem("v_stored")
            block = c1.enter_context(nc.Block())

            @block.sync
            def _(sp):
                def load_pos(c):
                    sp.dma_start(pos_sb[:, c % 2],
                                 pos_t[:, c * BANK:(c + 1) * BANK].rearrange("(k p) n -> p k n", p=P))\
                      .then_inc(pos_loaded[c % 2], 16)
                sp.dma_start(wr_sb[:, :, :], wr_t.rearrange("(k p) n -> p k n", p=P)).then_inc(w_loaded, 16)
                load_pos(0)
                load_pos(1)
                for dst, src in ((w_in_sb, w_in), (wq_sb, wq_t), (wk_sb, wk_t), (wv_sb, wv_t)):
                    sp.dma_start(dst[:, :, :], src.rearrange("(k p) n -> p k n", p=P)).then_inc(w_loaded, 16)
                for dst, src in ((w_out_sb, w_out), (ident_sb, ident), (fold_sb, fold), (iota_sb, iota)):
                    sp.dma_start(dst.ap(), src).then_inc(w_loaded, 16)
                with nc.allow_non_contiguous_dma(reason="512 biases"):
                    for i, b in enumerate((u_bias, v_bias)):
                        sp.dma_start(bias_sb[:, i, :], b.rearrange("(k p) -> p k", p=P)).then_inc(w_loaded, 16)
                for b in range(NB):
                    sp.dma_start(x_all[:, b * NI:(b + 1) * NI, :], x[b].rearrange("(n p) d -> p n d", p=P))\
                      .then_inc(x_loaded, 16)
                for s in stored + [v_stored]:
                    sp.sem_inc(s, 16)
                for c in range(NPC):
                    for m in range(KT):
                        sp.wait_ge(part3, KT * c + m + 1)
                        for b in range(NB):
                            sp.dma_start(pos_parts[:, (b * KT + m) * P:(b * KT + m + 1) * P,
                                                   c * BANK:(c + 1) * BANK].rearrange("s r n -> r s n"),
                                         part[:, m]).then_inc(stored[m], 8 * 2)
                    if c + 2 < NPC:
                        sp.wait_ge(projected, KT * (c + 1))
                        load_pos(c + 2)
                with sp.Fori(0, NB) as b:
                    with sp.Fori(0, GB) as q:
                        g = b * GB + q
                        for j in range(NSPLIT):
                            sp.wait_ge(part3, g * NSPLIT + (NPS + j + 1))
                            dst = (qu_parts, qv_parts, k_parts)[j // KT]
                            rows = bass.ds(b * (H * DH) + (j % KT) * P, P)
                            sp.dma_start(dst[:, rows, bass.ds(q * GT, GT)].rearrange("s r n -> r s n"), part[:, j])\
                              .then_inc(stored[j], 16)
                        sp.wait_ge(v_out, (g + 1) * TG)
                        sp.dma_start(v_heads[bass.ds(b * H, H), :, bass.ds(q * (TG * VW), TG * VW)]
                                     .rearrange("h p n -> p h n"),
                                     v_sb[:, :, :, :].rearrange("p h t w -> p h (t w)")).then_inc(v_stored, 16)
                for j in range(NSPLIT):
                    sp.wait_ge(stored[j], 16 * (1 + NG + (NB * NPC if j < KT else 0)))
                sp.wait_ge(v_stored, 16 * (1 + NG))

            @block.tensor
            def _(pe):
                pe.wait_ge(w_loaded, 16 * 11)
                for c in range(NPC):
                    pe.wait_ge(pos_loaded[c % 2], 16 * (c // 2 + 1))
                    for m in range(KT):
                        j = KT * c + m
                        if j >= 2:
                            pe.wait_ge(proj_out, j - 1)
                        for kt in range(KT):
                            last = pe.matmul(bank[2 + j % 2][:, :], lhsT=wr_sb[:, kt, m * P:(m + 1) * P],
                                             rhs=pos_sb[:, c % 2, kt, :], start=(kt == 0), stop=(kt == KT - 1))
                        last.then_inc(projected, 1)
                pe.wait_ge(proj_out, NPS)
                with pe.Fori(0, NB) as b:
                    with pe.Fori(0, GB) as q:
                        g = b * GB + q
                        ffn_pe(pe, B, S, g)
                        pe.wait_ge(normed2, g * TG + TG)
                        transpose_normed(pe, B, norm2_tp)
                        pe.wait_ge(norm2_t, g * KT + KT)
                        for i in range(NPJ):
                            w_sb, m = (wq_sb, wk_sb)[i // KT], i % KT
                            for kt in range(KT):
                                last = pe.matmul(bank[(2, 3, 5, 6)[i]][:, :], lhsT=w_sb[:, kt, m * P:(m + 1) * P],
                                                 rhs=B["norm_t"][:, kt, :], start=(kt == 0), stop=(kt == KT - 1))
                            last.then_inc(projected, 1)
                        for i in range(2):
                            for t in (2 * i, 2 * i + 1):
                                for kt in range(KT):
                                    last = pe.matmul(pairs((4, 7)[i], D)[:, t % 2, :],
                                                     lhsT=B["norm_t"][:, kt, t * P:(t + 1) * P],
                                                     rhs=wv_sb[:, kt, :], start=(kt == 0), stop=(kt == KT - 1))
                            last.then_inc(v_projected, 1)
                        pe.wait_ge(proj_out, g * NPJ + (NPS + NPJ))
                        pe.wait_ge(v_out, (g + 1) * TG)

            @block.scalar
            def _(act):
                act.wait_ge(w_loaded, 16 * 11)
                act.wait_ge(v_padded, 2)
                for j in range(NPS):
                    slot = j % KT
                    act.wait_ge(projected, j + 1)
                    if j >= KT:
                        act.wait_ge(rest1, j - KT + 1)
                    act.copy(proj[:, slot, :], bank[2 + slot][:, :]).then_inc(proj_out, 1)
                    act.wait_ge(proj_out, j + 1)
                    act.wait_ge(stored[slot], 16 * (NB * (j // KT) + 1))
                    act.copy(part[:, slot, 0, :], proj[:, slot, :]).then_inc(part1, 1)
                with act.Fori(0, NB) as b:
                    with act.Fori(0, GB) as q:
                        g = b * GB + q
                        ffn_act(act, B, S, g, 2 * g + 1)
                        root(act, B, S, 2 * g + 2)
                        for kt in range(KT):
                            act.wait_ge(norm2_tp, g * KT + (kt + 1))
                            act.copy(B["norm_t"][:, kt, :], bank[kt][:, :]).then_inc(norm2_t, 1)
                        act.wait_ge(rest1, g * NSPLIT + NPS)
                        for i in range(NPJ):
                            act.wait_ge(projected, g * NPJ + (NPS + i + 1))
                            act.copy(proj[:, i, :], bank[(2, 3, 5, 6)[i]][:, :]).then_inc(proj_out, 1)
                        for j in range(NSPLIT):
                            i = j % KT + (KT if j >= 2 * KT else 0)
                            act.wait_ge(proj_out, g * NPJ + (NPS + i + 1))
                            act.wait_ge(stored[j], 16 * (g + (1 + (NB * NPC if j < KT else 0))))
                            act.activation(part[:, j, 0, :], proj[:, i, :], ACT.Identity, scale=1.0,
                                           bias=bias_sb[:, j // KT, i:i + 1] if j < 2 * KT else 0.0)\
                               .then_inc(part1, 1)
                        for t in range(TG):
                            act.wait_ge(v_projected, 2 * g + (t // 2 + 1))
                            if t == 0:
                                act.wait_ge(v_stored, 16 * (g + 1))
                            act.copy(v_sb[:, :, t, 0:DH], by_head(pairs((4, 7)[t // 2], D)[:, t % 2, :]))\
                               .then_inc(v_out, 1)

            @block.vector
            def _(dve):
                def rest_1(n, slot, i, bias):
                    dve.wait_ge(part1, n + 1)
                    dve.scalar_tensor_tensor(rest[:, slot, :], proj[:, i, :], bias, part[:, slot, 0, :],
                                             ALU.add, ALU.subtract).then_inc(rest1, 1)
                dve.wait_ge(w_loaded, 16 * 11)
                for j in range(NPS):
                    if j >= KT:
                        dve.wait_ge(part3, j - KT + 1)
                    rest_1(j, j % KT, j % KT, 0.0)
                dve.wait_ge(part3, NPS)
                dve.wait_ge(x_loaded, 16 * NB)
                with dve.Fori(0, NB) as b:
                    with dve.Fori(0, GB) as q:
                        g = b * GB + q
                        base = g * NSTEP
                        ffn_dve(dve, B, S, g, base, 2 * g + 1, lambda t: by_head(x_all[:, b * NI + q * TG + t, :]),
                                lambda t: resid_tile(b, q, t))
                        wait_apart(dve, S["y"], (g + 1) * TG)
                        layer_norm(dve, B, S, base + FFN_STEPS, 2 * g + 2, lambda t: resid_tile(b, q, t), normed2)
                        for j in range(NSPLIT):
                            i = j % KT + (KT if j >= 2 * KT else 0)
                            dve.wait_ge(part3, g * NSPLIT + (NPS + j - (NSPLIT - 1)))
                            rest_1(g * NSPLIT + (NPS + j), j, i, bias_sb[:, j // KT, i:i + 1] if j < 2 * KT else 0.0)

            @block.gpsimd
            def _(pool):
                pool.memset(v_sb[:, :, :, DH:VW], 0.0).then_inc(v_padded, 1)
                pool.wait_ge(v_padded, 1)
                pool.memset(v_sb[:, :, :, DH:DH + 1], 1.0).then_inc(v_padded, 1)

                def parts_2_and_3(n, slot):
                    wait_apart(pool, rest1, n + 1)
                    pool.tensor_copy(part[:, slot, 1, :], rest[:, slot, :]).then_inc(part2, 1)
                    pool.wait_ge(part2, n + 1)
                    pool.tensor_tensor(part[:, slot, 2, :], rest[:, slot, :], part[:, slot, 1, :], ALU.subtract)\
                        .then_inc(part3, 1)
                for j in range(NPS):
                    parts_2_and_3(j, j % KT)
                with pool.Fori(0, NB) as b:
                    with pool.Fori(0, GB) as q:
                        for j in range(NSPLIT):
                            parts_2_and_3((b * GB + q) * NSPLIT + (NPS + j), j)

        with ExitStack() as c2:
            def s2(name, shape, dt=F32):
                return c2.enter_context(nc.sbuf_tensor(name, shape, dt))
            NU = 2
            NT = NU * NI
            STEPS = HEADS // NU
            NK = L // BANK
            NP = NK + 1
            qu = [s2(f"qu{u}", [STACK, L], BF16) for u in range(NU)]
            qv = [s2(f"qv{u}", [STACK, L + 16], BF16) for u in range(NU)]
            ks = [s2(f"ks{u}", [STACK, L], BF16) for u in range(NU)]
            pos = [s2(f"pos{u}", [STACK, NPOS], BF16) for u in range(NU)]
            vs = [s2(f"vs{u}", [P, NI, VW]) for u in range(NU)]
            unshifted = s2("unshifted", [P, SLOTS, WIN])
            score = s2("score", [P, SCORES, L])
            top4 = s2("top4", [P, SCORES, NK])
            minus_max = s2("minus_max", [P, SCORES])
            PSL = 4
            prob_t = s2("prob_t", [P, PSL, BANK])
            FT = 4
            acc_sb = s2("acc_sb", [P, FT * P])
            rden = s2("rden", [P, FT])
            head_out = s2("head_out", [P, FT, DH])
            AC, POS, PT, ACC, FIN = bank[0:2], bank[2:4], bank[4:6], bank[6], bank[7]
            operands, tail_zeroed = [sem(f"operands{u}") for u in range(NU)], sem("tail_zeroed")
            ac_full, ac_used = sem("ac_full"), sem("ac_used")
            pos_full, pos_out = sem("pos_full"), sem("pos_out")
            written = [sem(f"written{i}") for i in range(SLOTS)]
            read_back = [sem(f"read_back{i}") for i in range(SLOTS)]
            scored, exped = sem("scored"), sem("exped")
            pt_full, pt_out, pv_done = sem("pt_full"), sem("pt_out"), sem("pv_done")  
            acc_full, acc_out, fin_full, fin_used = sem("acc_full"), sem("acc_out"), sem("fin_full"), sem("fin_used")
            normalised = sem("normalised")
            block = c2.enter_context(nc.Block())
            NLOAD = 4 * len(Q_PARTS) + 1

            POS_AHEAD, AC_AHEAD, EXP_AHEAD = 6, 2, 1

            def slot_uses(step, k):
                return step * (NT // SLOTS) + k // SLOTS

            def steps(eng, body):
                with eng.Fori(0, STEPS - 1) as step:
                    body(step, False)
                body(STEPS - 1, True)

            @block.gpsimd
            def _(pool):
                for u in range(NU):
                    pool.memset(qv[u][:, L:L + 16], 0.0).then_inc(tail_zeroed, 1)
                with pool.Fori(0, STEPS) as step:
                    for u in range(NU):
                        hd = step * NU + u
                        pool.wait_ge(fin_used, hd * (NI // FT) + (NI // FT + 1))
                        for dst, src, order, n in ((qv[u], qv_parts, Q_PARTS, L), (pos[u], pos_parts, K_PARTS, NPOS),
                                                   (qu[u], qu_parts, Q_PARTS, L), (ks[u], k_parts, K_PARTS, L)):
                            for i, which in enumerate(order):
                                pool.dma_start(dst[i * DH:(i + 1) * DH, 0:n],
                                               src[which, bass.ds(hd * DH, DH), :]).then_inc(operands[u], 16)
                        pool.dma_start(vs[u][:, :, :].rearrange("p t w -> p (t w)"),
                                       v_heads[bass.ds(hd, 1), :, :].rearrange("o p n -> p (o n)"))\
                            .then_inc(operands[u], 16)

            @block.sync
            def _(sp):
                for i in range(SLOTS):
                    sp.sem_inc(written[i], 16)
                    sp.sem_inc(read_back[i], 16)

                def write(step, k):
                    g, i = step * NT + k, k % SLOTS
                    sp.wait_ge(pos_out, g * NP + (NP + 2))
                    sp.wait_ge(read_back[i], slot_uses(step, k) * 16 + 16)
                    sp.dma_start(shift_dram.ap()[i], unshifted[:, i, :]).then_inc(written[i], 16)

                def read(step, k):
                    g, i = step * NT + k, k % SLOTS
                    wait_apart(sp, pt_full, NK * (g + 1))
                    sp.wait_ge(written[i], slot_uses(step, k) * 16 + 32)
                    sp.dma_start(score[:, k % SCORES, :],
                                 bass.AP(shift_dram, i * P * WIN + P - 1, [[WIN - 1, P], [1, L]]))\
                      .then_inc(read_back[i], 16)

                def body(step, last):
                    for k in range(NT):
                        if not (last and k + 1 == NT):
                            write(step, k + 1)
                        read(step, k)
                write(0, 0)
                steps(sp, body)
                for i in range(SLOTS):
                    sp.wait_ge(read_back[i], 16 * (STEPS * NT // SLOTS + 1))

            @block.tensor
            def _(pe):
                pe.wait_ge(tail_zeroed, NU)

                def positions(step, k, c):
                    u, i, g = k // NI % NU, k % NI, step * NT + k
                    if i == 0 and c == 0:
                        pe.wait_ge(operands[u], (step_of(step, k) + 1) * (16 * NLOAD))
                    pe.wait_ge(pos_out, g * NP + (c + 1))
                    dst, first = POS[(k * NP + c) % 2], c * BANK
                    width = min(BANK, WIN - first)
                    split = min(max((i + 1) * P - first, 0), width)
                    at = (NI - 1 - i) * P + first
                    for lo, hi, ahead in ((0, split, 0), (split, width, 1)):
                        if hi > lo:
                            last = pe.matmul(dst[:, lo:hi], lhsT=qv[u][:, i * P + ahead:(i + 1) * P + ahead],
                                             rhs=pos[u][:, at + lo:at + hi], start=True, stop=True)
                    last.then_inc(pos_full, 1)

                def step_of(step, k):
                    return step + k // NT

                def content(step, k, c):
                    u, i, g = k // NI % NU, k % NI, step * NT + k
                    pe.wait_ge(ac_used, g * NK + (c + 1))
                    pe.matmul(AC[c % 2][:, :], lhsT=qu[u][:, i * P:(i + 1) * P],
                              rhs=ks[u][:, c * BANK:(c + 1) * BANK], start=True, stop=True).then_inc(ac_full, 1)

                def turn(step, k, c):
                    g = step * NT + k
                    pe.wait_ge(exped, 2 * g + (c // 2 + 1))
                    pe.wait_ge(pt_out, g * NK + (c + 1))
                    for t in range(4):
                        last = pe.matmul(PT[c % 2][:, t * P:(t + 1) * P],
                                         lhsT=score[:, k % SCORES, c * BANK + t * P:c * BANK + (t + 1) * P],
                                         rhs=ident_sb[:, :], is_transpose=True, start=True, stop=True)
                    last.then_inc(pt_full, 1)

                def weigh(step, k, c):
                    u, g, f = k // NI % NU, step * NT + k, k % FT
                    if c == 0 and f == 0:
                        pe.wait_ge(acc_out, finished(step, k) + 1)
                    pe.wait_ge(pt_out, g * NK + (c + 3))
                    for t in range(4):
                        last = pe.matmul(ACC[t * VW:(t + 1) * VW, f * P:(f + 1) * P], lhsT=vs[u][:, 4 * c + t, :],
                                         rhs=prob_t[:, c % PSL, t * P:(t + 1) * P], start=(c == 0),
                                         stop=(c == NK - 1))
                    last.then_inc(pv_done, 1)
                def finished(step, k):
                    return step * (NT // FT) + k // FT

                def finish(step, k):
                    n = finished(step, k)
                    pe.wait_ge(acc_out, n + 2)
                    pe.wait_ge(fin_used, n + (1 + NU * NI // FT))
                    for f in range(FT):
                        last = pe.matmul(FIN[:, f * VW:(f + 1) * VW], lhsT=acc_sb[:, f * P:(f + 1) * P],
                                         rhs=fold_sb[:, :], start=True, stop=True)
                    last.then_inc(fin_full, 1)

                def body(step, last):
                    for k in range(NT):
                        for c in range(NK):
                            if not (last and k + POS_AHEAD >= NT):
                                positions(step, k + POS_AHEAD, c)
                            if not (last and k + AC_AHEAD >= NT):
                                content(step, k + AC_AHEAD, c)
                            turn(step, k, c)
                            if c:
                                weigh(step, k, c - 1)
                        if not (last and k + POS_AHEAD >= NT):
                            positions(step, k + POS_AHEAD, NP - 1)
                        weigh(step, k, NK - 1)
                        if k % FT == FT - 1:
                            finish(step, k)

                for k in range(POS_AHEAD):
                    for c in range(NP):
                        positions(0, k, c)
                for k in range(AC_AHEAD):
                    for c in range(NK):
                        content(0, k, c)
                steps(pe, body)

            @block.scalar
            def _(act):
                act.sem_inc(pos_out, 2)

                def take(step, k, c):
                    g = step * NT + k
                    if c == 0:
                        act.wait_ge(written[k % SLOTS], slot_uses(step, k) * 16 + 16)
                    act.wait_ge(pos_full, g * NP + (c + 1))
                    lo, hi = c * BANK, min((c + 1) * BANK, WIN)
                    act.copy(unshifted[:, k % SLOTS, lo:hi], POS[(k * NP + c) % 2][:, 0:hi - lo]).then_inc(pos_out, 1)

                def exponentials(step, k, half):
                    if half == 0:
                        act.wait_ge(scored, step * NT + (k + 1))
                    cols = score[:, k % SCORES, half * (L // 2):(half + 1) * (L // 2)]
                    act.activation(cols, cols, ACT.Exp, bias=minus_max[:, k % SCORES:k % SCORES + 1], scale=1.0)\
                       .then_inc(exped, 1)

                def body(step, last):
                    for k in range(NT):
                        for c in range(NP):
                            if not (last and k + POS_AHEAD >= NT):
                                take(step, k + POS_AHEAD, c)
                            if c in (1, 3) and not (last and k + EXP_AHEAD >= NT):
                                exponentials(step, k + EXP_AHEAD, c // 2)
                for k in range(POS_AHEAD):
                    for c in range(NP):
                        take(0, k, c)
                for half in range(2):
                    exponentials(0, 0, half)
                steps(act, body)

            @block.vector
            def _(dve):
                for s, n in ((ac_used, 2), (pt_full, NK * (SCORES - 1)), (pt_out, 2), (pv_done, PSL),
                             (acc_out, 1), (fin_used, 1 + NU * NI // FT)):
                    dve.sem_inc(s, n)

                def add(step, k, c):
                    g, i = step * NT + k, k % SCORES
                    if c == 0:
                        dve.wait_ge(read_back[k % SLOTS], slot_uses(step, k) * 16 + 32)
                    wait_apart(dve, ac_full, g * NK + (c + 1))
                    cols = slice(c * BANK, (c + 1) * BANK)
                    dve.tensor_tensor_reduce(score[:, i, cols], AC[c % 2][:, :], score[:, i, cols], SCALE,
                                             NEG, ALU.add, ALU.max, top4[:, i, c:c + 1]).then_inc(ac_used, 1)

                def maximum(step, k):
                    g, i = step * NT + k, k % SCORES
                    dve.wait_ge(ac_used, (g + 1) * NK + 2)
                    dve.tensor_reduce(minus_max[:, i:i + 1], top4[:, i, :], AX.X, ALU.max, negate=True)\
                       .then_inc(scored, 1)

                def take(step, k, c):
                    n = (step * NT + k) * NK + c
                    dve.wait_ge(pt_full, n + (NK * (SCORES - 1) + 1))
                    dve.wait_ge(pv_done, n + 1)
                    dve.tensor_copy(prob_t[:, c % PSL, :], PT[c % 2][:, :]).then_inc(pt_out, 1)

                def finish(step, k):
                    u = k // NI
                    n = step * (NT // FT) + k // FT
                    dve.wait_ge(pv_done, (step * NT + (k + 1)) * NK + PSL)
                    dve.tensor_copy(acc_sb[:, :], ACC[:, :]).then_inc(acc_out, 1)
                    dve.wait_ge(fin_full, n + 1)
                    fin = FIN[:, 0:FT * VW].rearrange("p (f w) -> p f w", w=VW)
                    dve.reciprocal(rden[:, :], fin[:, :, DH]).then_inc(normalised, 1)
                    dve.wait_ge(normalised, n * 2 + 1)
                    dve.tensor_tensor(head_out[:, :, :], fin[:, :, 0:DH],
                                      rden[:, :].rearrange("p (f o) -> p f o", o=1).to_broadcast([P, FT, DH]),
                                      ALU.mult).then_inc(normalised, 1)
                    dve.wait_ge(normalised, n * 2 + 2)
                    i = k % NI
                    res = resid[:, bass.ds(step * NU + u, 1), i - FT + 1:i + 1, :].rearrange("p o t d -> p (o t) d")
                    dve.tensor_tensor(res, res, head_out[:, :, :], ALU.add).then_inc(fin_used, 1)

                def body(step, last):
                    for k in range(NT):
                        for c in range(NK):
                            if not (last and k + AC_AHEAD >= NT):
                                add(step, k + AC_AHEAD, c)
                            take(step, k, c)
                        if not (last and k + AC_AHEAD >= NT):
                            maximum(step, k + AC_AHEAD)
                        if k % FT == FT - 1:
                            finish(step, k)
                for k in range(AC_AHEAD):
                    for c in range(NK):
                        add(0, k, c)
                    maximum(0, k)
                steps(dve, body)

        with ExitStack() as c3:
            B = ffn_buffers(c3, "two")
            S = ffn_sems("two")
            y_sb = c3.enter_context(nc.sbuf_tensor("y_sb", [P, TG, D], F32))
            y_stored = sem("y_stored")
            block = c3.enter_context(nc.Block())

            @block.sync
            def _(sp):
                sp.sem_inc(y_stored, 16)
                with sp.Fori(0, NG) as g:
                    sp.wait_ge(S["y"], (g + 1) * TG)
                    sp.dma_start(out.rearrange("b (n p) d -> p (b n) d", p=P)[:, bass.ds(g * TG, TG), :],
                                 y_sb[:, :, :]).then_inc(y_stored, 16)
                sp.wait_ge(y_stored, 16 * (NG + 1))

            @block.tensor
            def _(pe):
                with pe.Fori(0, NG) as g:
                    ffn_pe(pe, B, S, g)

            @block.scalar
            def _(act):
                with act.Fori(0, NG) as g:
                    ffn_act(act, B, S, g, g + 1)

            @block.vector
            def _(dve):
                with dve.Fori(0, NB) as b:
                    with dve.Fori(0, GB) as q:
                        g = b * GB + q
                        ffn_dve(dve, B, S, g, g * FFN_STEPS, g + 1, lambda t: resid_tile(b, q, t),
                                lambda t: by_head(y_sb[:, t, :]), y_stored)


def position_table(length, width):
    import numpy as np
    power = 10000.0 ** (np.arange(0, width, 2) / width)
    inv_freq = np.float32(1.0) / power.astype(np.float32)
    angle = np.arange(-(length - 1), length, dtype=np.float32)[:, None] * inv_freq[None, :]
    table = np.zeros((2 * length - 1, width), np.float32)
    table[:, 0::2], table[:, 1::2] = np.sin(angle), np.cos(angle)
    rows = np.concatenate([table[length - 1:], np.zeros((1, width), np.float32), table[:length - 1]])
    return np.ascontiguousarray(rows.T)


def kernel(**inputs):
    import numpy as np
    import concourse.bacc as bacc
    from concourse.bass_utils import run_bass_kernel_spmd

    g = {k: np.asarray(v) for k, v in inputs.items()}
    x = g["L0_attn_w"]
    nb, length, width = x.shape
    experts, rank = g["L0_ffn_A"].shape[0], g["L0_ffn_A"].shape[2]
    hidden = g["L0_ffn_A"].transpose(1, 0, 2).reshape(width, experts * rank)
    fold = np.tile(np.eye(32, dtype=np.float32), (4, 1))
    arrays = {
        "x": x,
        "wq_t": g["L0_attn_Wq"].T, "wk_t": g["L0_attn_Wk"].T, "wv_t": g["L0_attn_Wv"].T, "wr_t": g["L0_attn_Wr"].T,
        "u_bias": g["L0_attn_u_bias"].reshape(-1), "v_bias": g["L0_attn_v_bias"].reshape(-1),
        "w_in": np.concatenate([g["L0_ffn_Wg"], hidden], axis=1),
        "w_out": g["L0_ffn_B"].reshape(experts * rank, width),
        "pos_t": position_table(length, width),
        "ident": np.eye(128, dtype=np.float32), "fold": fold,
        "iota": np.broadcast_to(np.arange(experts, dtype=np.float32), (128, 4, experts)),
    }
    nc = bacc.Bacc("TRN2", target_bir_lowering=False, num_devices=1)
    arrays = {n: np.ascontiguousarray(a) for n, a in arrays.items()}
    args = {n: nc.dram_tensor(n, a.shape, mybir.dt.from_np(a.dtype), kind="ExternalInput").ap()
            for n, a in arrays.items()}
    out = nc.dram_tensor("out", x.shape, F32, kind="ExternalOutput").ap()
    build_program(nc, out=out, **args)
    got = run_bass_kernel_spmd(nc, [arrays], core_ids=[0])
    return got.results[0]["out"]
```

```python
from contextlib import ExitStack

import concourse.bass as bass
from concourse import mybir

ALU = mybir.AluOpType
ACT = mybir.ActivationFunctionType
AX = mybir.AxisListType
F32 = mybir.dt.float32
BF16 = mybir.dt.bfloat16
U32 = mybir.dt.uint32

P = 128
Q_PARTS = (0, 0, 0, 1, 1, 2)
K_PARTS = (0, 1, 2, 0, 1, 0)
EPS = 1e-5


def build_program(nc, x, wq_t, wk_t, wv_t, wr_t, u_bias, v_bias, w_in, w_out, pos_t, ident, fold, iota, out):
    NB, L, D = x.shape
    E = iota.shape[2]
    ER = w_out.shape[0]
    R = ER // E
    H, DH = 16, D // 16
    KT = D // P
    NI = L // P
    NPOS = 2 * L
    WIN = L + P
    TG = 4
    GT = TG * P
    GB = L // GT
    NG = NB * GB
    HEADS = NB * H
    STACK = len(Q_PARTS) * DH
    VW = 32
    SCALE = float(DH) ** -0.5
    NEG = -3.0e38
    BANK = 512
    assert (P, D, DH, KT, ER) == (128, 256, 16, 2, 128)

    ctx = ExitStack()
    with ctx:
        def sb(name, shape, dt=F32):
            return ctx.enter_context(nc.sbuf_tensor(name, shape, dt))

        def sem(name):
            return ctx.enter_context(nc.semaphore(name))

        bank = [ctx.enter_context(nc.psum_tensor(f"bank{i}", [P, BANK], F32)) for i in range(8)]

        qu_parts = nc.dram_tensor("qu_parts", (3, HEADS * DH, L), BF16, kind="Internal").ap()
        qv_parts = nc.dram_tensor("qv_parts", (3, HEADS * DH, L), BF16, kind="Internal").ap()
        k_parts = nc.dram_tensor("k_parts", (3, HEADS * DH, L), BF16, kind="Internal").ap()
        pos_parts = nc.dram_tensor("pos_parts", (3, HEADS * DH, NPOS), BF16, kind="Internal").ap()
        v_heads = nc.dram_tensor("v_heads", (HEADS, P, NI * VW), F32, kind="Internal").ap()
        SLOTS = 8
        RING = 8
        UNSHIFTED = 3
        MOVED = 4
        QUAD = 32
        MWIN = L + QUAD
        SCORES = RING + MOVED
        shift_dram = nc.dram_tensor("shift_dram", (SLOTS, P, WIN), F32, kind="Internal")

        x_one = nc.dram_tensor("x_one", (NB, L, D), F32, kind="Internal").ap()
        attended = nc.dram_tensor("attended", (HEADS, P, NI * DH), F32, kind="Internal").ap()

        ident_sb = sb("ident_sb", [P, P])
        fold_sb = sb("fold_sb", [P, VW])
        iota_sb = sb("iota_sb", [P, TG, E])
        w_loaded = sem("w_loaded")

        def token_tiles(ap):
            return ap.rearrange("b (n p) d -> p (b n) d", p=P)

        def by_head(ap):
            return ap.rearrange("p (h d) -> p h d", h=H)

        NORM_STEPS = 2 * TG + 1
        FFN_STEPS = NORM_STEPS + 3 * TG + 7

        LANES = 2
        NPAIR = GB // LANES

        def in_step(*lanes):
            while lanes:
                lanes = [lane for lane in lanes if next(lane, "ended") != "ended"]

        def ffn_buffers(c, tag, lane):
            def s(name, shape, dt=F32):
                return c.enter_context(nc.sbuf_tensor(f"{name}_{tag}", shape, dt))
            return dict(
                bank=bank[4 * lane:4 * lane + 4],
                norm=s("normed", [P, TG, D]), norm_t=s("normed_t", [P, KT, GT]),
                stats=s("stats", [P, TG, 6]), mean_var=s("mean_var", [P, TG, 2]), rstd=s("rstd", [P, TG]),
                var=s("var", [P, TG]), root=s("root", [P, TG]),
                logits=s("logits", [P, TG, E]), top=s("top", [P, TG, 8]), top_i=s("top_i", [P, TG, 8], U32),
                top_f=s("top_f", [P, TG, 2]), diff=s("diff", [P, TG]), ex=s("ex", [P, TG]),
                den=s("den", [P, TG]), w=s("w_top", [P, 2, TG]), mask=s("mask", [P, 2, TG, E]),
                gate=s("gate", [P, TG, E]), hw=s("hw", [P, TG, ER]), hw_t=s("hw_t", [P, GT]))

        def ffn_sems(tag):
            names = ("var", "rooted", "normed", "norm_tp", "norm_t", "hidden", "diff", "exp", "gated", "gated_tp", "gated_t",
                     "ffn", "chain", "y")
            return {n: sem(f"{n}_{tag}") for n in names}

        def wait_apart(eng, semaphore, count):
            eng.wait_ge(semaphore, count)
            eng.nop(nofuse=True)

        def layer_norm(dve, B, S, base, no, tile, normed):
            chain = S["chain"]
            for t in range(TG):
                dve.bn_stats(B["stats"][:, t, :], tile(t)).then_inc(chain, 1)
            for t in range(TG):
                wait_apart(dve, chain, base + (t + 1))
                dve.bn_aggr(B["mean_var"][:, t, :], B["stats"][:, t, :]).then_inc(chain, 1)
            yield
            dve.wait_ge(chain, base + 2 * TG)
            dve.tensor_scalar(B["var"][:, :], B["mean_var"][:, :, 1], EPS, None, ALU.add).then_inc(S["var"], 1)
            yield
            dve.wait_ge(S["rooted"], no)
            dve.reciprocal(B["rstd"][:, :], B["root"][:, :]).then_inc(chain, 1)
            yield
            dve.wait_ge(chain, base + (2 * TG + 1))
            for t in range(TG):
                dve.tensor_scalar(by_head(B["norm"][:, t, :]), tile(t), B["mean_var"][:, t, 0:1],
                                  B["rstd"][:, t:t + 1], ALU.subtract, ALU.mult).then_inc(normed, 1)

        def pairs(one_bank, width):
            return one_bank[:, 0:2 * width].rearrange("p (t c) -> p t c", t=2)

        def root(act, B, S, no):
            act.wait_ge(S["var"], no)
            act.activation(B["root"][:, :], B["var"][:, :], ACT.Sqrt).then_inc(S["rooted"], 1)

        def ffn_dve(dve, B, S, g, base, no, tile, y_tile, y_free=None):
            chain = S["chain"]
            yield from layer_norm(dve, B, S, base, no, tile, S["normed"])
            yield
            n = base + NORM_STEPS
            dve.wait_ge(S["hidden"], g + 1)
            for i in range(2):
                dve.tensor_copy(B["logits"][:, 2 * i:2 * i + 2, :], pairs(B["bank"][2 + i], E + ER)[:, :, 0:E])\
                   .then_inc(chain, 1)
            yield
            wait_apart(dve, chain, n + 2)
            for t in range(TG):
                dve.max(B["top"][:, t, :], B["logits"][:, t, :]).then_inc(chain, 1)
            n = n + 2
            yield
            dve.wait_ge(chain, n + TG)
            dve.tensor_tensor(B["diff"][:, :], B["top"][:, :, 1], B["top"][:, :, 0], ALU.subtract)\
               .then_inc(S["diff"], 1)
            for t in range(TG):
                dve.max_index(B["top_i"][:, t, :], B["top"][:, t, :], B["logits"][:, t, :]).then_inc(chain, 1)
            n = n + 2 * TG
            yield
            dve.wait_ge(chain, n)
            dve.tensor_copy(B["top_f"][:, :, :], B["top_i"][:, :, 0:2]).then_inc(chain, 1)
            yield
            dve.wait_ge(S["exp"], g + 1)
            dve.tensor_scalar(B["den"][:, :], B["ex"][:, :], 2.0, 2.0, ALU.mult, ALU.add).then_inc(chain, 1)
            yield
            dve.wait_ge(chain, n + 2)
            dve.reciprocal(B["w"][:, 0, :], B["den"][:, :]).then_inc(chain, 1)
            for j in range(2):
                dve.tensor_tensor(B["mask"][:, j], iota_sb[:, :, :],
                                  B["top_f"][:, :, j:j + 1].to_broadcast([P, TG, E]), ALU.is_equal)\
                   .then_inc(chain, 1)
            yield
            dve.wait_ge(chain, n + 5)
            dve.tensor_tensor(B["w"][:, 1, :], B["w"][:, 0, :], B["ex"][:, :], ALU.mult).then_inc(chain, 1)
            yield
            dve.wait_ge(chain, n + 6)
            for j in range(2):
                wj = B["w"][:, j, :].rearrange("p (t o) -> p t o", o=1).to_broadcast([P, TG, E])
                dve.tensor_tensor(B["mask"][:, j], B["mask"][:, j], wj, ALU.mult).then_inc(chain, 1)
            yield
            dve.wait_ge(chain, n + 8)
            dve.tensor_tensor(B["gate"][:, :, :], B["mask"][:, 0], B["mask"][:, 1], ALU.add).then_inc(chain, 1)
            yield
            dve.wait_ge(chain, n + 9)
            for t in range(TG):
                dve.tensor_tensor(B["hw"][:, t, :].rearrange("p (e r) -> p e r", e=E),
                                  pairs(B["bank"][2 + t // 2], E + ER)[:, t % 2, E:E + ER]
                                  .rearrange("p (e r) -> p e r", e=E),
                                  B["gate"][:, t, :].rearrange("p (e o) -> p e o", o=1).to_broadcast([P, E, R]),
                                  ALU.mult).then_inc(S["gated"], 1)
            yield
            if y_free is not None:
                dve.wait_ge(y_free, 16 * (g + 1))
            dve.wait_ge(S["ffn"], g + 1)
            for t in range(TG):
                dve.tensor_tensor(y_tile(t), by_head(pairs(B["bank"][2 + t // 2], D)[:, t % 2, :]), tile(t), ALU.add)\
                   .then_inc(S["y"], 1)

        def ffn_act(act, B, S, g, no):
            root(act, B, S, no)
            yield
            for kt in range(KT):
                act.wait_ge(S["norm_tp"], g * KT + (kt + 1))
                act.copy(B["norm_t"][:, kt, :], B["bank"][kt][:, :]).then_inc(S["norm_t"], 1)
            yield
            act.wait_ge(S["diff"], g + 1)
            act.activation(B["ex"][:, :], B["diff"][:, :], ACT.Exp).then_inc(S["exp"], 1)
            yield
            act.wait_ge(S["gated_tp"], g + 1)
            act.copy(B["hw_t"][:, :], B["bank"][0][:, :]).then_inc(S["gated_t"], 1)

        def transpose_normed(pe, B, transposed):
            for kt in range(KT):
                for t in range(TG):
                    last = pe.matmul(B["bank"][kt][:, t * P:(t + 1) * P], lhsT=B["norm"][:, t, kt * P:(kt + 1) * P],
                                     rhs=ident_sb[:, :], is_transpose=True, start=True, stop=True)
                last.then_inc(transposed, 1)

        def ffn_pe(pe, B, S, g, w_in_sb, w_out_sb):
            pe.wait_ge(S["normed"], g * TG + TG)
            transpose_normed(pe, B, S["norm_tp"])
            yield
            pe.wait_ge(S["norm_t"], g * KT + KT)
            for t in range(TG):
                for kt in range(KT):
                    last = pe.matmul(pairs(B["bank"][2 + t // 2], E + ER)[:, t % 2, :],
                                     lhsT=B["norm_t"][:, kt, t * P:(t + 1) * P], rhs=w_in_sb[:, kt, :],
                                     start=(kt == 0), stop=(kt == KT - 1))
            last.then_inc(S["hidden"], 1)
            yield
            pe.wait_ge(S["gated"], g * TG + TG)
            for t in range(TG):
                last = pe.matmul(B["bank"][0][:, t * P:(t + 1) * P], lhsT=B["hw"][:, t, :], rhs=ident_sb[:, :],
                                 is_transpose=True, start=True, stop=True)
            last.then_inc(S["gated_tp"], 1)
            yield
            pe.wait_ge(S["gated_t"], g + 1)
            for t in range(TG):
                last = pe.matmul(pairs(B["bank"][2 + t // 2], D)[:, t % 2, :], lhsT=B["hw_t"][:, t * P:(t + 1) * P],
                                 rhs=w_out_sb[:, :], start=True, stop=True)
            last.then_inc(S["ffn"], 1)

        with ExitStack() as c1:

            def s1(name, shape, dt=F32):
                return c1.enter_context(nc.sbuf_tensor(name, shape, dt))
            x_all = s1("x_all", [P, NB * NI, D])
            w_in_sb, w_out_sb = s1("w_in_sb", [P, KT, E + ER]), s1("w_out_sb", [P, D])
            wq_sb, wk_sb, wv_sb, wr_sb = (s1(n, [P, KT, D]) for n in ("wq_sb", "wk_sb", "wv_sb", "wr_sb"))
            bias_sb = s1("bias_sb", [P, 2, KT])
            pos_sb = s1("pos_sb", [P, 2, KT, BANK])
            NPJ = 2 * KT
            NSPLIT = 3 * KT
            NPC = NPOS // BANK
            NSTEP = NORM_STEPS + FFN_STEPS
            LB, LS = [], []
            for lane in range(LANES):
                tag = f"one{lane}"
                LB.append(dict(ffn_buffers(c1, tag, lane), x_one=s1(f"x_one_sb{lane}", [P, TG, D]),
                               v=s1(f"v_sb{lane}", [P, H, TG, VW]), proj=s1(f"proj{lane}", [P, NPJ, BANK]),
                               part=s1(f"part{lane}", [P, NSPLIT, 3, BANK], BF16),
                               rest=s1(f"rest{lane}", [P, NSPLIT, BANK])))
                names = ("normed2", "norm2_tp", "norm2_t", "projected", "proj_out", "v_projected", "v_out",
                         "part1", "rest1", "part2", "part3", "v_padded", "v_stored", "x_one_stored")
                LS.append(dict(ffn_sems(tag), **{n: sem(f"{n}_{lane}") for n in names},
                               stored=[sem(f"stored{i}_{lane}") for i in range(NSPLIT)]))
            x_loaded = sem("x_loaded")
            pos_loaded = [sem(f"pos_loaded{i}") for i in range(2)]
            block = c1.enter_context(nc.Block())

            assert LANES == KT

            @block.sync
            def _(sp):
                def load_pos(c):
                    sp.dma_start(pos_sb[:, c % 2],
                                 pos_t[:, c * BANK:(c + 1) * BANK].rearrange("(k p) n -> p k n", p=P))\
                        .then_inc(pos_loaded[c % 2], 16)
                sp.dma_start(wr_sb[:, :, :], wr_t.rearrange("(k p) n -> p k n", p=P)).then_inc(w_loaded, 16)
                load_pos(0)
                load_pos(1)
                for dst, src in ((w_in_sb, w_in), (wq_sb, wq_t), (wk_sb, wk_t), (wv_sb, wv_t)):
                    sp.dma_start(dst[:, :, :], src.rearrange("(k p) n -> p k n", p=P)).then_inc(w_loaded, 16)
                for dst, src in ((w_out_sb, w_out), (ident_sb, ident), (fold_sb, fold), (iota_sb, iota)):
                    sp.dma_start(dst.ap(), src).then_inc(w_loaded, 16)
                with nc.allow_non_contiguous_dma(reason="512 biases"):
                    for i, b in enumerate((u_bias, v_bias)):
                        sp.dma_start(bias_sb[:, i, :], b.rearrange("(k p) -> p k", p=P)).then_inc(w_loaded, 16)
                for b in range(NB):
                    sp.dma_start(x_all[:, b * NI:(b + 1) * NI, :], x[b].rearrange("(n p) d -> p n d", p=P))\
                      .then_inc(x_loaded, 16)
                for S in LS:
                    for s in S["stored"] + [S["v_stored"], S["x_one_stored"]]:
                        sp.sem_inc(s, 16)
                for c in range(NPC):
                    for m, (B, S) in enumerate(zip(LB, LS)):
                        sp.wait_ge(S["part3"], c + 1)
                        for b in range(NB):
                            sp.dma_start(pos_parts[:, (b * KT + m) * P:(b * KT + m + 1) * P,
                                                   c * BANK:(c + 1) * BANK].rearrange("s r n -> r s n"),
                                         B["part"][:, 0]).then_inc(S["stored"][0], 16)
                    if c + 2 < NPC:
                        for S in LS:
                            sp.wait_ge(S["projected"], c + 1)
                        load_pos(c + 2)

                def stores(lane, b, q, n):
                    B, S = LB[lane], LS[lane]
                    sp.wait_ge(S["y"], (n + 1) * TG)
                    sp.dma_start(token_tiles(x_one)[:, bass.ds((b * GB + q) * TG, TG), :], B["x_one"][:, :, :])\
                      .then_inc(S["x_one_stored"], 16)
                    yield
                    for j in range(NSPLIT):
                        sp.wait_ge(S["part3"], n * NSPLIT + (NPC + j + 1))
                        dst = (qu_parts, qv_parts, k_parts)[j // KT]
                        rows = bass.ds(b * (H * DH) + (j % KT) * P, P)
                        sp.dma_start(dst[:, rows, bass.ds(q * GT, GT)].rearrange("s r n -> r s n"), B["part"][:, j])\
                          .then_inc(S["stored"][j], 16)
                        yield
                    sp.wait_ge(S["v_out"], (n + 1) * TG)
                    sp.dma_start(v_heads[bass.ds(b * H, H), :, bass.ds(q * (TG * VW), TG * VW)]
                                 .rearrange("h p n -> p h n"),
                                 B["v"][:, :, :, :].rearrange("p h t w -> p h (t w)")).then_inc(S["v_stored"], 16)
                with sp.Fori(0, NB) as b:
                    with sp.Fori(0, NPAIR) as pair:
                        in_step(*(stores(lane, b, pair * LANES + lane, b * NPAIR + pair) for lane in range(LANES)))
                for S in LS:
                    for j in range(NSPLIT):
                        sp.wait_ge(S["stored"][j], 16 * (1 + NB * NPAIR + (NB * NPC if j == 0 else 0)))
                    sp.wait_ge(S["v_stored"], 16 * (1 + NB * NPAIR))
                    sp.wait_ge(S["x_one_stored"], 16 * (1 + NB * NPAIR))

            @block.tensor
            def _(pe):
                pe.wait_ge(w_loaded, 16 * 11)
                for c in range(NPC):
                    pe.wait_ge(pos_loaded[c % 2], 16 * (c // 2 + 1))
                    for m, (B, S) in enumerate(zip(LB, LS)):
                        if c:
                            pe.wait_ge(S["proj_out"], c)
                        for kt in range(KT):
                            last = pe.matmul(B["bank"][2][:, :], lhsT=wr_sb[:, kt, m * P:(m + 1) * P],
                                             rhs=pos_sb[:, c % 2, kt, :], start=(kt == 0), stop=(kt == KT - 1))
                        last.then_inc(S["projected"], 1)
                for S in LS:
                    pe.wait_ge(S["proj_out"], NPC)

                def group(lane, n):
                    B, S = LB[lane], LS[lane]
                    yield from ffn_pe(pe, B, S, n, w_in_sb, w_out_sb)
                    yield
                    pe.wait_ge(S["normed2"], n * TG + TG)
                    transpose_normed(pe, B, S["norm2_tp"])
                    yield
                    pe.wait_ge(S["norm2_t"], n * KT + KT)
                    for i in range(NPJ):
                        w_sb, m = (wq_sb, wk_sb)[i // KT], i % KT
                        for kt in range(KT):
                            last = pe.matmul(B["bank"][(2, 3, 0, 1)[i]][:, :], lhsT=w_sb[:, kt, m * P:(m + 1) * P],
                                             rhs=B["norm_t"][:, kt, :], start=(kt == 0), stop=(kt == KT - 1))
                        last.then_inc(S["projected"], 1)
                    yield
                    pe.wait_ge(S["proj_out"], n * NPJ + (NPC + KT))
                    for i in range(2):
                        for t in (2 * i, 2 * i + 1):
                            for kt in range(KT):
                                last = pe.matmul(pairs(B["bank"][2 + i], D)[:, t % 2, :],
                                                 lhsT=B["norm_t"][:, kt, t * P:(t + 1) * P],
                                                 rhs=wv_sb[:, kt, :], start=(kt == 0), stop=(kt == KT - 1))
                        last.then_inc(S["v_projected"], 1)
                    yield
                    pe.wait_ge(S["proj_out"], n * NPJ + (NPC + NPJ))
                    pe.wait_ge(S["v_out"], (n + 1) * TG)
                with pe.Fori(0, NB * NPAIR) as n:
                    in_step(*(group(lane, n) for lane in range(LANES)))

            @block.scalar
            def _(act):
                act.wait_ge(w_loaded, 16 * 11)
                for S in LS:
                    act.wait_ge(S["v_padded"], 2)
                for c in range(NPC):
                    for m, (B, S) in enumerate(zip(LB, LS)):
                        act.wait_ge(S["projected"], c + 1)
                        if c:
                            act.wait_ge(S["rest1"], c)
                        act.copy(B["proj"][:, 0, :], B["bank"][2][:, :]).then_inc(S["proj_out"], 1)
                        act.wait_ge(S["proj_out"], c + 1)
                        act.wait_ge(S["stored"][0], 16 * (NB * c + 1))
                        act.copy(B["part"][:, 0, 0, :], B["proj"][:, 0, :]).then_inc(S["part1"], 1)

                def group(lane, n):
                    B, S = LB[lane], LS[lane]
                    yield from ffn_act(act, B, S, n, 2 * n + 1)
                    yield
                    root(act, B, S, 2 * n + 2)
                    yield
                    for kt in range(KT):
                        act.wait_ge(S["norm2_tp"], n * KT + (kt + 1))
                        act.copy(B["norm_t"][:, kt, :], B["bank"][kt][:, :]).then_inc(S["norm2_t"], 1)
                    yield
                    act.wait_ge(S["rest1"], n * NSPLIT + NPC)
                    for i in range(NPJ):
                        act.wait_ge(S["projected"], n * NPJ + (NPC + i + 1))
                        act.copy(B["proj"][:, i, :], B["bank"][(2, 3, 0, 1)[i]][:, :]).then_inc(S["proj_out"], 1)
                    yield
                    for j in range(NSPLIT):
                        i = j % KT + (KT if j >= 2 * KT else 0)
                        act.wait_ge(S["proj_out"], n * NPJ + (NPC + i + 1))
                        act.wait_ge(S["stored"][j], 16 * (n + (1 + (NB * NPC if j == 0 else 0))))
                        act.activation(B["part"][:, j, 0, :], B["proj"][:, i, :], ACT.Identity, scale=1.0,
                                       bias=bias_sb[:, j // KT, i:i + 1] if j < 2 * KT else 0.0)\
                            .then_inc(S["part1"], 1)
                        yield
                    for t in range(TG):
                        act.wait_ge(S["v_projected"], 2 * n + (t // 2 + 1))
                        if t == 0:
                            act.wait_ge(S["v_stored"], 16 * (n + 1))
                        act.copy(B["v"][:, :, t, 0:DH], by_head(pairs(B["bank"][2 + t // 2], D)[:, t % 2, :]))\
                           .then_inc(S["v_out"], 1)
                with act.Fori(0, NB * NPAIR) as n:
                    in_step(*(group(lane, n) for lane in range(LANES)))

            @block.vector
            def _(dve):
                def rest_1(B, S, n, slot, i, bias):
                    dve.wait_ge(S["part1"], n + 1)
                    dve.scalar_tensor_tensor(B["rest"][:, slot, :], B["proj"][:, i, :], bias, B["part"][:, slot, 0, :],
                                             ALU.add, ALU.subtract).then_inc(S["rest1"], 1)
                dve.wait_ge(w_loaded, 16 * 11)
                for c in range(NPC):
                    for B, S in zip(LB, LS):
                        if c:
                            dve.wait_ge(S["part3"], c)
                        rest_1(B, S, c, 0, 0, 0.0)
                for S in LS:
                    dve.wait_ge(S["part3"], NPC)
                dve.wait_ge(x_loaded, 16 * NB)

                def group(lane, b, q, n):
                    B, S = LB[lane], LS[lane]
                    base = n * NSTEP

                    def y_tile(t):
                        return by_head(B["x_one"][:, t, :])
                    yield from ffn_dve(dve, B, S, n, base, 2 * n + 1,
                                       lambda t: by_head(x_all[:, b * NI + q * TG + t, :]), y_tile, S["x_one_stored"])
                    yield
                    wait_apart(dve, S["y"], (n + 1) * TG)
                    yield from layer_norm(dve, B, S, base + FFN_STEPS, 2 * n + 2, y_tile, S["normed2"])
                    yield
                    for j in range(NSPLIT):
                        i = j % KT + (KT if j >= 2 * KT else 0)
                        dve.wait_ge(S["part3"], n * NSPLIT + (NPC + j - (NSPLIT - 1)))
                        rest_1(B, S, n * NSPLIT + (NPC + j), j, i,
                               bias_sb[:, j // KT, i:i + 1] if j < 2 * KT else 0.0)
                        yield
                with dve.Fori(0, NB) as b:
                    with dve.Fori(0, NPAIR) as pair:
                        in_step(*(group(lane, b, pair * LANES + lane, b * NPAIR + pair) for lane in range(LANES)))

            @block.gpsimd
            def _(pool):
                for B, S in zip(LB, LS):
                    pool.memset(B["v"][:, :, :, DH:VW], 0.0).then_inc(S["v_padded"], 1)
                for B, S in zip(LB, LS):
                    pool.wait_ge(S["v_padded"], 1)
                    pool.memset(B["v"][:, :, :, DH:DH + 1], 1.0).then_inc(S["v_padded"], 1)

                def parts_2_and_3(B, S, n, slot):
                    wait_apart(pool, S["rest1"], n + 1)
                    pool.tensor_copy(B["part"][:, slot, 1, :], B["rest"][:, slot, :]).then_inc(S["part2"], 1)
                    pool.wait_ge(S["part2"], n + 1)
                    pool.tensor_tensor(B["part"][:, slot, 2, :], B["rest"][:, slot, :], B["part"][:, slot, 1, :],
                                       ALU.subtract).then_inc(S["part3"], 1)
                for c in range(NPC):
                    for B, S in zip(LB, LS):
                        parts_2_and_3(B, S, c, 0)
                with pool.Fori(0, NB * NPAIR) as n:
                    for j in range(NSPLIT):
                        for B, S in zip(LB, LS):
                            parts_2_and_3(B, S, n * NSPLIT + (NPC + j), j)

        with ExitStack() as c2:
            def s2(name, shape, dt=F32):
                return c2.enter_context(nc.sbuf_tensor(name, shape, dt))
            NU = 2
            NT = NU * NI
            STEPS = HEADS // NU
            NK = L // BANK
            NP = NK + 1
            qu = [s2(f"qu{u}", [STACK, L], BF16) for u in range(NU)]
            qv = [s2(f"qv{u}", [STACK, L + 16], BF16) for u in range(NU)]
            ks = [s2(f"ks{u}", [STACK, L], BF16) for u in range(NU)]
            pos = [s2(f"pos{u}", [STACK, NPOS], BF16) for u in range(NU)]
            vs = [s2(f"vs{u}", [P, NI, VW]) for u in range(NU)]
            unshifted = s2("unshifted", [P, UNSHIFTED, WIN])
            to_move = s2("to_move", [P, MOVED, MWIN])
            score = s2("score", [P, SCORES, L])
            top4 = s2("top4", [P, SCORES, NK])
            minus_max = s2("minus_max", [P, SCORES])
            PSL = 2
            prob_t = s2("prob_t", [P, PSL, BANK])
            FT = 4
            acc_sb = s2("acc_sb", [P, FT * P])
            rden = s2("rden", [P, FT])
            head_out = s2("head_out", [P, NU, NI, DH])
            AC, POS, PT, ACC, FIN = bank[0:2], bank[2:4], bank[4:6], bank[6], bank[7]
            pos_operands = [sem(f"pos_operands{u}") for u in range(NU)]
            content_operands = [sem(f"content_operands{u}") for u in range(NU)]
            tail_zeroed = sem("tail_zeroed")
            ac_full, ac_used = sem("ac_full"), sem("ac_used")
            pos_full, pos_out = sem("pos_full"), sem("pos_out")
            written = [sem(f"written{i}") for i in range(SLOTS)]
            read_back = [sem(f"read_back{i}") for i in range(SLOTS)]
            scored, exped = sem("scored"), sem("exped")
            pt_full, pt_out, pv_done = sem("pt_full"), sem("pt_out"), sem("pv_done")  
            moved, output_stored, output_free = sem("moved"), sem("output_stored"), sem("output_free")
            acc_full, acc_out, fin_full, fin_used = sem("acc_full"), sem("acc_out"), sem("fin_full"), sem("fin_used")
            inverted = sem("inverted")
            block = c2.enter_context(nc.Block())
            NLOAD = 2 * len(Q_PARTS)

            POS_AHEAD, AC_AHEAD = 11, 1
            LOAD_AT = (7, 8, 9, 10)
            BOUNCED = NI - MOVED
            MADE = (0, 1, 2, 3, 12, 4, 13, 5, 6, 14, 7, 8, 15, 9, 10, 11)
            MADE_MOVED = MADE.index(NI - 1) + 1
            assert sorted(MADE) == list(range(NI)) and NU * BOUNCED % SLOTS == 0

            def head_of(step, k):
                return step * NU + k // NI

            def bounce(k):
                return k // NI * BOUNCED + k % NI

            def slot_uses(step, n):
                return step * (NU * BOUNCED // SLOTS) + n // SLOTS

            def score_slot(k):
                return bounce(k) % RING if k % NI < BOUNCED else RING + k % NI - BOUNCED

            def steps(eng, body):
                with eng.Fori(0, STEPS - 1) as step:
                    body(step, False)
                body(STEPS - 1, True)

            @block.gpsimd
            def _(pool):
                for u in range(NU):
                    pool.memset(qv[u][:, L:L + 16], 0.0).then_inc(tail_zeroed, 1)

                def store(hd, u):
                    wait_apart(pool, fin_used, hd * (NI // FT) + (NI // FT + 1))
                    pool.dma_start(attended[bass.ds(hd, 1), :, :].rearrange("o p n -> p (o n)"),
                                   head_out[:, u].rearrange("p t d -> p (t d)")).then_inc(output_stored, 16)
                    wait_apart(pool, output_stored, hd * 16 + 16)
                    pool.sem_inc(output_free, 1)

                def move(hd):
                    wait_apart(pool, pt_full, hd * (NI * NK) + NK * SCORES)
                    wait_apart(pool, pos_out, hd * (NI * NP) + (MADE_MOVED * NP + 2))
                    for s in range(QUAD):
                        pool.dma_start(score[s::QUAD, RING:SCORES, :],
                                       to_move[s::QUAD, :, QUAD - 1 - s:QUAD - 1 - s + L]).then_inc(moved, 16)
                move(0)
                with pool.Fori(0, STEPS - 1) as step:
                    for u in range(NU):
                        hd = step * NU + u
                        store(hd, u)
                        move(hd + 1)
                store(HEADS - 2, 0)
                move(HEADS - 1)
                store(HEADS - 1, 1)

            @block.sync
            def _(sp):
                for i in range(SLOTS):
                    sp.sem_inc(written[i], 16)
                    sp.sem_inc(read_back[i], 16)

                def write(step, k):
                    n, made = bounce(k), k // NI * NI + MADE.index(k % NI)
                    slot = n % SLOTS
                    sp.wait_ge(pos_out, step * (NT * NP) + (made * NP + NP + 2))
                    sp.wait_ge(read_back[slot], slot_uses(step, n) * 16 + 16)
                    sp.dma_start(shift_dram.ap()[slot], unshifted[:, n % UNSHIFTED, :]).then_inc(written[slot], 16)

                def read(step, k):
                    n = bounce(k)
                    slot = n % SLOTS
                    back = RING if k % NI >= RING else RING + MOVED
                    wait_apart(sp, pt_full, step * (NT * NK) + NK * (SCORES + k - back + 1))
                    sp.wait_ge(written[slot], slot_uses(step, n) * 16 + 32)
                    sp.dma_start(score[:, score_slot(k), :],
                                 bass.AP(shift_dram, slot * P * WIN + P - 1, [[WIN - 1, P], [1, L]]))\
                      .then_inc(read_back[slot], 16)

                def load_operands(hd, u, which):
                    dst, src, order, n = ((pos[u], pos_parts, K_PARTS, NPOS), (qv[u], qv_parts, Q_PARTS, L),
                                          (qu[u], qu_parts, Q_PARTS, L), (ks[u], k_parts, K_PARTS, L))[which]
                    loaded = (pos_operands if which < 2 else content_operands)[u]
                    for i, part in enumerate(order):
                        sp.dma_start(dst[i * DH:(i + 1) * DH, 0:n],
                                     src[part, bass.ds(hd * DH, DH), :]).then_inc(loaded, 16)
                    if which == len(LOAD_AT) - 1:
                        sp.dma_start(vs[u][:, :, :].rearrange("p t w -> p (t w)"),
                                     v_heads[bass.ds(hd, 1), :, :].rearrange("o p n -> p (o n)"))\
                            .then_inc(loaded, 16)

                bounced = [k for k in range(NT) if k % NI < BOUNCED]

                def body(step, last):
                    for n, k in enumerate(bounced):
                        if n + 1 < len(bounced):
                            write(step, bounced[n + 1])
                        elif not last:
                            write(step, NT)
                        read(step, k)
                        u = k // NI
                        if k % NI in LOAD_AT and not (last and u == NU - 1):
                            if k % NI == LOAD_AT[0]:
                                sp.wait_ge(fin_used, (step * NU + u) * (NI // FT) + 1)
                            load_operands(step * NU + (u + 1), (u + 1) % NU, LOAD_AT.index(k % NI))
                for which in range(len(LOAD_AT)):
                    load_operands(0, 0, which)
                write(0, 0)
                steps(sp, body)
                for slot in range(SLOTS):
                    sp.wait_ge(read_back[slot], 16 * (HEADS * BOUNCED // SLOTS + 1))

            @block.tensor
            def _(pe):
                pe.wait_ge(tail_zeroed, NU)

                def positions(step, n, c):
                    u, i, g = n // NI % NU, MADE[n % NI], step * NT + n
                    if n % NI == 0 and c == 0:
                        pe.wait_ge(pos_operands[u], (step_of(step, n) + 1) * (16 * NLOAD))
                    pe.wait_ge(pos_out, g * NP + (c + 1))
                    dst, first = POS[(n * NP + c) % 2], c * BANK
                    rows = P if i < BOUNCED else QUAD
                    width = min(BANK, L + rows - first)
                    for row in range(0, P, rows):
                        moves = P - rows - row
                        split = min(max((i + 1) * P - moves - first, 0), width)
                        at = (NI - 1 - i) * P + moves + first
                        for lo, hi, ahead in ((0, split, 0), (split, width, 1)):
                            if hi > lo:
                                q0 = i * P + row + ahead
                                last = pe.matmul(dst[row:row + rows, lo:hi], lhsT=qv[u][:, q0:q0 + rows],
                                                 rhs=pos[u][:, at + lo:at + hi], start=True, stop=True)
                    last.then_inc(pos_full, 1)

                def step_of(step, k):
                    return step + k // NT

                def content(step, k, c):
                    u, i, g = k // NI % NU, k % NI, step * NT + k
                    if i == 0 and c == 0:
                        pe.wait_ge(content_operands[u], (step_of(step, k) + 1) * (16 * (NLOAD + 1)))
                    pe.wait_ge(ac_used, g * NK + (c + 1))
                    pe.matmul(AC[c % 2][:, :], lhsT=qu[u][:, i * P:(i + 1) * P],
                              rhs=ks[u][:, c * BANK:(c + 1) * BANK], start=True, stop=True).then_inc(ac_full, 1)

                def turn(step, k, c):
                    g = step * NT + k
                    pe.wait_ge(exped, 2 * g + (c // 2 + 1))
                    pe.wait_ge(pt_out, g * NK + (c + 1))
                    for t in range(4):
                        last = pe.matmul(PT[c % 2][:, t * P:(t + 1) * P],
                                         lhsT=score[:, score_slot(k), c * BANK + t * P:c * BANK + (t + 1) * P],
                                         rhs=ident_sb[:, :], is_transpose=True, start=True, stop=True)
                    last.then_inc(pt_full, 1)

                def weigh(step, k, c):
                    u, g, f = k // NI % NU, step * NT + k, k % FT
                    if c == 0 and f == 0:
                        pe.wait_ge(acc_out, finished(step, k) + 1)
                    pe.wait_ge(pt_out, g * NK + (c + 3))
                    for t in range(4):
                        last = pe.matmul(ACC[t * VW:(t + 1) * VW, f * P:(f + 1) * P], lhsT=vs[u][:, 4 * c + t, :],
                                         rhs=prob_t[:, c % PSL, t * P:(t + 1) * P], start=(c == 0),
                                         stop=(c == NK - 1))
                    last.then_inc(pv_done, 1)
                def finished(step, k):
                    return step * (NT // FT) + k // FT

                def finish(step, k):
                    n = finished(step, k)
                    pe.wait_ge(acc_out, n + 2)
                    pe.wait_ge(fin_used, n + 1)
                    for f in range(FT):
                        last = pe.matmul(FIN[:, f * VW:(f + 1) * VW], lhsT=acc_sb[:, f * P:(f + 1) * P],
                                         rhs=fold_sb[:, :], start=True, stop=True)
                    last.then_inc(fin_full, 1)

                def body(step, last):
                    for k in range(NT):
                        for c in range(NK):
                            make = not (last and k + POS_AHEAD >= NT)
                            if make and c>=0:
                                positions(step, k + POS_AHEAD, c)
                            turn(step, k, c)
                            ahead, chunk = k + AC_AHEAD + (c + 1) // NK, (c + 1) % NK
                            if not (last and ahead >= NT):
                                content(step, ahead, chunk)
                            if c:
                                weigh(step, k, c - 1)
                            if c == 1 and k % FT == 0 and k:
                                finish(step, k - 1)
                        if not (last and k + POS_AHEAD >= NT):
                            positions(step, k + POS_AHEAD, NP - 1)
                        weigh(step, k, NK - 1)
                        if k == NT - 1:
                            finish(step, k)

                for k in range(POS_AHEAD):
                    for c in range(NP):
                        positions(0, k, c)
                for k in range(AC_AHEAD):
                    for c in range(NK):
                        content(0, k, c)
                content(0, AC_AHEAD, 0)
                steps(pe, body)

            @block.scalar
            def _(act):
                act.sem_inc(pos_out, 2)

                def take(step, n, c):
                    i, k = MADE[n % NI], n // NI * NI + MADE[n % NI]
                    m = bounce(k)
                    if c == 0 and i < BOUNCED:
                        act.wait_ge(written[(m - UNSHIFTED) % SLOTS], slot_uses(step, m - UNSHIFTED) * 16 + 32)
                    if c == 0 and i == BOUNCED and n >= NI:
                        act.wait_ge(moved, head_of(step, k) * (16 * QUAD))
                    act.wait_ge(pos_full, step * (NT * NP) + (n * NP + c + 1))
                    dst, width = (unshifted[:, m % UNSHIFTED, :], WIN) if i < BOUNCED else \
                        (to_move[:, i - BOUNCED, :], MWIN)
                    lo, hi = c * BANK, min((c + 1) * BANK, width)
                    act.copy(dst[:, lo:hi], POS[(n * NP + c) % 2][:, 0:hi - lo]).then_inc(pos_out, 1)

                def exponentials(step, k, half):
                    slot = score_slot(k)
                    if half == 0:
                        act.wait_ge(scored, step * NT + (k + 1))
                    cols = score[:, slot, half * (L // 2):(half + 1) * (L // 2)]
                    act.activation(cols, cols, ACT.Exp, bias=minus_max[:, slot:slot + 1], scale=1.0)\
                       .then_inc(exped, 1)

                def body(step, last):
                    for k in range(NT):
                        for c in range(NP):
                            if not (last and k + POS_AHEAD >= NT):
                                take(step, k + POS_AHEAD, c)
                            if c == 0:
                                exponentials(step, k, 1)
                            if c == 2 and not (last and k + AC_AHEAD >= NT):
                                exponentials(step, k + AC_AHEAD, 0)
                for n in range(POS_AHEAD):
                    for c in range(NP):
                        take(0, n, c)
                exponentials(0, 0, 0)
                steps(act, body)

            @block.vector
            def _(dve):
                for s, n in ((ac_used, 2), (pt_full, NK * SCORES), (pt_out, 2), (pv_done, PSL),
                             (acc_out, 1), (fin_used, 1), (output_free, NU)):
                    dve.sem_inc(s, n)

                def add(step, k, c):
                    g, i = step * NT + k, score_slot(k)
                    if c == 0 and k % NI < BOUNCED:
                        dve.wait_ge(read_back[bounce(k) % SLOTS], slot_uses(step, bounce(k)) * 16 + 32)
                    if c == 0 and k % NI == BOUNCED:
                        dve.wait_ge(moved, head_of(step, k) * (16 * QUAD) + 16 * QUAD)
                    wait_apart(dve, ac_full, g * NK + (c + 1))
                    cols = slice(c * BANK, (c + 1) * BANK)
                    dve.tensor_tensor_reduce(score[:, i, cols], AC[c % 2][:, :], score[:, i, cols], SCALE,
                                             NEG, ALU.add, ALU.max, top4[:, i, c:c + 1]).then_inc(ac_used, 1)

                def maximum(step, k):
                    g, i = step * NT + k, score_slot(k)
                    dve.wait_ge(ac_used, (g + 1) * NK + 2)
                    dve.tensor_reduce(minus_max[:, i:i + 1], top4[:, i, :], AX.X, ALU.max, negate=True)\
                       .then_inc(scored, 1)

                def take(step, k, c):
                    n = (step * NT + k) * NK + c
                    dve.wait_ge(pt_full, n + (NK * SCORES + 1))
                    dve.wait_ge(pv_done, n + 1)
                    dve.tensor_copy(prob_t[:, c % PSL, :], PT[c % 2][:, :]).then_inc(pt_out, 1)

                def sums_out(step, k):
                    dve.wait_ge(pv_done, (step * NT + (k + 1)) * NK + PSL)
                    dve.tensor_copy(acc_sb[:, :], ACC[:, :]).then_inc(acc_out, 1)

                def finish(step, k):
                    u, i, n = k // NI, k % NI, step * (NT // FT) + k // FT
                    dve.wait_ge(fin_full, n + 1)
                    fin = FIN[:, 0:FT * VW].rearrange("p (f w) -> p f w", w=VW)
                    dve.reciprocal(rden[:, :], fin[:, :, DH]).then_inc(inverted, 1)
                    if i == FT - 1:
                        dve.wait_ge(output_free, head_of(step, k) + 1)
                    dve.wait_ge(inverted, n + 1)
                    dve.tensor_tensor(head_out[:, u, i - FT + 1:i + 1, :], fin[:, :, 0:DH],
                                      rden[:, :].rearrange("p (f o) -> p f o", o=1).to_broadcast([P, FT, DH]),
                                      ALU.mult).then_inc(fin_used, 1)

                def late(k):
                    return k % FT == FT - 1 and k < NT - 1

                def body(step, last):
                    for k in range(NT):
                        ahead = not (last and k + AC_AHEAD >= NT)
                        for c in range(NK // 2):
                            if ahead:
                                add(step, k + AC_AHEAD, c)
                            if c == 0 and k and late(k - 1):
                                sums_out(step, k - 1)
                            take(step, k, c)
                        if ahead:
                            for c in range(NK // 2, NK):
                                add(step, k + AC_AHEAD, c)
                            maximum(step, k + AC_AHEAD)
                        if k and late(k - 1):
                            finish(step, k - 1)
                        for c in range(NK // 2, NK):
                            take(step, k, c)
                        if k == NT - 1:
                            sums_out(step, k)
                            finish(step, k)
                for k in range(AC_AHEAD):
                    for c in range(NK):
                        add(0, k, c)
                    maximum(0, k)
                steps(dve, body)

        with ExitStack() as c3:
            def s3(name, shape):
                return c3.enter_context(nc.sbuf_tensor(name, shape, F32))
            LB = [dict(ffn_buffers(c3, f"two{lane}", lane), y=s3(f"y_sb{lane}", [P, TG, D])) for lane in range(LANES)]
            LS = [dict(ffn_sems(f"two{lane}"), y_stored=sem(f"y_stored{lane}")) for lane in range(LANES)]
            w_in_sb, w_out_sb = s3("w_in_sb2", [P, KT, E + ER]), s3("w_out_sb2", [P, D])
            x_all = s3("x_one_all", [P, NB * NI, D])
            attended_sb = s3("attended_sb", [P, HEADS, NI, DH])
            x_loaded, w_loaded2 = sem("x_one_loaded"), sem("w_loaded2")
            block = c3.enter_context(nc.Block())

            @block.sync
            def _(sp):
                for b in range(NB):
                    sp.dma_start(x_all[:, b * NI:(b + 1) * NI, :], token_tiles(x_one)[:, b * NI:(b + 1) * NI, :])\
                      .then_inc(x_loaded, 16)
                    sp.dma_start(attended_sb[:, b * H:(b + 1) * H].rearrange("p h t d -> p h (t d)"),
                                 attended[b * H:(b + 1) * H].rearrange("h p n -> p h n")).then_inc(x_loaded, 16)
                sp.dma_start(w_in_sb[:, :, :], w_in.rearrange("(k p) n -> p k n", p=P)).then_inc(w_loaded2, 16)
                sp.dma_start(w_out_sb[:, :], w_out).then_inc(w_loaded2, 16)
                for S in LS:
                    sp.sem_inc(S["y_stored"], 16)
                with sp.Fori(0, NB * NPAIR) as n:
                    for lane, (B, S) in enumerate(zip(LB, LS)):
                        sp.wait_ge(S["y"], (n + 1) * TG)
                        sp.dma_start(token_tiles(out)[:, bass.ds((n * LANES + lane) * TG, TG), :], B["y"][:, :, :])\
                          .then_inc(S["y_stored"], 16)
                for S in LS:
                    sp.wait_ge(S["y_stored"], 16 * (NB * NPAIR + 1))

            @block.tensor
            def _(pe):
                pe.wait_ge(w_loaded2, 16 * 2)
                with pe.Fori(0, NB * NPAIR) as n:
                    in_step(*(ffn_pe(pe, B, S, n, w_in_sb, w_out_sb) for B, S in zip(LB, LS)))

            @block.scalar
            def _(act):
                with act.Fori(0, NB * NPAIR) as n:
                    in_step(*(ffn_act(act, B, S, n, n + 1) for B, S in zip(LB, LS)))

            @block.vector
            def _(dve):
                dve.wait_ge(x_loaded, 16 * 2 * NB)

                def group(lane, b, q, n):
                    B, S = LB[lane], LS[lane]
                    base = n * (FFN_STEPS + TG) + TG

                    def x_tile(t):
                        return by_head(x_all[:, b * NI + q * TG + t, :])
                    for t in range(TG):
                        dve.tensor_tensor(x_tile(t), x_tile(t), attended_sb[:, bass.ds(b * H, H), q * TG + t, :],
                                          ALU.add).then_inc(S["chain"], 1)
                    yield
                    wait_apart(dve, S["chain"], base)
                    yield from ffn_dve(dve, B, S, n, base, n + 1, x_tile, lambda t: by_head(B["y"][:, t, :]),
                                       S["y_stored"])
                with dve.Fori(0, NB) as b:
                    with dve.Fori(0, NPAIR) as pair:
                        in_step(*(group(lane, b, pair * LANES + lane, b * NPAIR + pair) for lane in range(LANES)))


def position_table(length, width):
    import numpy as np
    power = 10000.0 ** (np.arange(0, width, 2) / width)
    inv_freq = np.float32(1.0) / power.astype(np.float32)
    angle = np.arange(-(length - 1), length, dtype=np.float32)[:, None] * inv_freq[None, :]
    table = np.zeros((2 * length - 1, width), np.float32)
    table[:, 0::2], table[:, 1::2] = np.sin(angle), np.cos(angle)
    rows = np.concatenate([table[length - 1:], np.zeros((1, width), np.float32), table[:length - 1]])
    return np.ascontiguousarray(rows.T)


def kernel(**inputs):
    import numpy as np
    import concourse.bacc as bacc
    from concourse.bass_utils import run_bass_kernel_spmd

    g = {k: np.asarray(v) for k, v in inputs.items()}
    x = g["L0_attn_w"]
    nb, length, width = x.shape
    experts, rank = g["L0_ffn_A"].shape[0], g["L0_ffn_A"].shape[2]
    hidden = g["L0_ffn_A"].transpose(1, 0, 2).reshape(width, experts * rank)
    fold = np.tile(np.eye(32, dtype=np.float32), (4, 1))
    arrays = {
        "x": x,
        "wq_t": g["L0_attn_Wq"].T, "wk_t": g["L0_attn_Wk"].T, "wv_t": g["L0_attn_Wv"].T, "wr_t": g["L0_attn_Wr"].T,
        "u_bias": g["L0_attn_u_bias"].reshape(-1), "v_bias": g["L0_attn_v_bias"].reshape(-1),
        "w_in": np.concatenate([g["L0_ffn_Wg"], hidden], axis=1),
        "w_out": g["L0_ffn_B"].reshape(experts * rank, width),
        "pos_t": position_table(length, width),
        "ident": np.eye(128, dtype=np.float32), "fold": fold,
        "iota": np.broadcast_to(np.arange(experts, dtype=np.float32), (128, 4, experts)),
    }
    nc = bacc.Bacc("TRN2", target_bir_lowering=False, num_devices=1)
    arrays = {n: np.ascontiguousarray(a) for n, a in arrays.items()}
    args = {n: nc.dram_tensor(n, a.shape, mybir.dt.from_np(a.dtype), kind="ExternalInput").ap()
            for n, a in arrays.items()}
    out = nc.dram_tensor("out", x.shape, F32, kind="ExternalOutput").ap()
    build_program(nc, out=out, **args)
    got = run_bass_kernel_spmd(nc, [arrays], core_ids=[0])
    return got.results[0]["out"]
```
